# Optimizing a Trainium2 kernel written in Bass

```python
import numpy as np
import jax
import jax.numpy as jnp

def _softmax(x, axis=-1):
    return jax.nn.softmax(x, axis=axis)

def _gelu(x):
    return jax.nn.gelu(x, approximate=True)

def _silu(x):
    return jax.nn.silu(x)

def _sigmoid(x):
    return jax.nn.sigmoid(x)

def _layernorm(x, axis=-1, eps=1e-05):
    m = jnp.mean(x, axis=axis, keepdims=True)
    v = jnp.var(x, axis=axis, keepdims=True)
    return (x - m) / jnp.sqrt(v + eps)

def _scatter_add(tgt, idx, src, axis=0):
    return tgt.at[idx].add(src)

def _segment_sum(src, seg, n):
    return jax.ops.segment_sum(src, seg, n)
kernel_name = 'mk_adaln_ffn_d1_seqx_r8_1e8ca2'

def setup_inputs(seed: int=0):
    np.random.seed(seed)
    _w = jnp.asarray

    def _rec_inputs():
        import jax
        import jax.numpy as jnp
        _rk = jax.random.key(seed)
        x = -7.109e-05 + 0.9999 * jax.random.normal(jax.random.fold_in(_rk, 1), (32, 32, 256), jnp.float32)
        _lenS = 32 - jax.random.randint(jax.random.fold_in(_rk, 7), (32,), 0, max(1, 32 // 4) + 1, jnp.int32)
        _lenS2 = 32 - jax.random.randint(jax.random.fold_in(_rk, 8), (32,), 0, max(1, 32 // 4) + 1, jnp.int32)
        itok_B_1_198 = jax.random.randint(jax.random.fold_in(_rk, 11), (32,), 1, 199, jnp.int32)
        return (x, itok_B_1_198)
    x, itok_B_1_198 = _rec_inputs()

    def _L0_cond_setup():
        import jax, jax.numpy as jnp
        import numpy as np
        B, C, T = (128, 32, 256)
        S, D = (200, 32)
        key = jax.random.key(seed)
        k1, k2, k3 = jax.random.split(key, 3)
        x = jax.random.normal(k1, (B, C, T), dtype=jnp.float32)
        conditions = jax.random.randint(k2, (B,), 0, S, dtype=jnp.int64)
        weights = jax.random.normal(k3, (S, C, D), dtype=jnp.float32) / jnp.sqrt(jnp.float32(C))
        return {'x': x, 'conditions': conditions, 'weights': weights}
    _L0_cond_all = _L0_cond_setup()
    _L0_cond_in = {k: v for k, v in _L0_cond_all.items() if k in ('weights',)}
    del _L0_cond_all

    def _L0_ffn_setup():
        import jax, jax.numpy as jnp
        import numpy as np
        DIM = 256
        HID = 128
        E = 8
        K = 2
        SHID = HID * 1
        INIT = 0.02
        key = jax.random.key(seed)
        ks = jax.random.split(key, 9)
        return {'x': jax.random.normal(ks[0], (2, 128, DIM), jnp.float32), 'expert_bias': jnp.zeros((E,), jnp.float32), 'gate_w': jax.random.normal(ks[1], (E, DIM), jnp.float32) * INIT, 'w1': jax.random.normal(ks[2], (E, HID, DIM), jnp.float32) * INIT, 'w2': jax.random.normal(ks[3], (E, DIM, HID), jnp.float32) * INIT, 'w3': jax.random.normal(ks[4], (E, HID, DIM), jnp.float32) * INIT, 'sw1': jax.random.normal(ks[5], (SHID, DIM), jnp.float32) * INIT, 'sw2': jax.random.normal(ks[6], (DIM, SHID), jnp.float32) * INIT, 'sw3': jax.random.normal(ks[7], (SHID, DIM), jnp.float32) * INIT}
    _L0_ffn_all = _L0_ffn_setup()
    _L0_ffn_in = {k: v for k, v in _L0_ffn_all.items() if k in ('expert_bias', 'gate_w', 'w1', 'w2', 'w3', 'sw1', 'sw2', 'sw3')}
    del _L0_ffn_all
    return {'x': x, 'itok_B_1_198': itok_B_1_198, 'L0_cond_weights': _L0_cond_in['weights'], 'L0_ffn_expert_bias': _L0_ffn_in['expert_bias'], 'L0_ffn_gate_w': _L0_ffn_in['gate_w'], 'L0_ffn_w1': _L0_ffn_in['w1'], 'L0_ffn_w2': _L0_ffn_in['w2'], 'L0_ffn_w3': _L0_ffn_in['w3'], 'L0_ffn_sw1': _L0_ffn_in['sw1'], 'L0_ffn_sw2': _L0_ffn_in['sw2'], 'L0_ffn_sw3': _L0_ffn_in['sw3']}

def reference(x, itok_B_1_198, L0_cond_weights, L0_ffn_expert_bias, L0_ffn_gate_w, L0_ffn_w1, L0_ffn_w2, L0_ffn_w3, L0_ffn_sw1, L0_ffn_sw2, L0_ffn_sw3):
    import jax
    import jax.numpy as jnp

    def _L0_cond_ref(x, conditions, weights):
        import jax, jax.numpy as jnp
        import numpy as np
        B, C, T = (128, 32, 256)
        S, D = (200, 32)
        w = weights[conditions]
        return jnp.einsum('bct,bcd->bdt', x, w)

    def _L0_ffn_ref(x, expert_bias, gate_w, w1, w2, w3, sw1, sw2, sw3):
        import jax, jax.numpy as jnp
        import numpy as np
        DIM = 256
        HID = 128
        E = 8
        K = 2
        SHID = HID * 1
        INIT = 0.02
        B, S, D = x.shape
        xf = x.reshape(-1, D)
        N = xf.shape[0]
        scores = jax.nn.sigmoid((xf @ gate_w.T).astype(jnp.float32))
        _, sel = jax.lax.top_k(scores + expert_bias[None, :], K)
        top_scores = jnp.take_along_axis(scores, sel, axis=1)
        flat_exp = sel.reshape(-1)
        order = jnp.argsort(flat_exp, stable=True)
        sorted_exp = flat_exp[order]
        tok_idx = order // K
        sc_sorted = top_scores.reshape(-1)[order]
        rin = xf[tok_idx] * sc_sorted[:, None].astype(x.dtype)
        out_sorted = jnp.zeros_like(rin)
        for e in range(E):
            m = (sorted_exp == e)[:, None].astype(rin.dtype)
            h = jax.nn.silu(rin @ w1[e].T) * (rin @ w3[e].T)
            out_sorted = out_sorted + m * (h @ w2[e].T)
        routed = jnp.zeros((N, D), x.dtype).at[tok_idx].add(out_sorted)
        shared = jax.nn.silu(xf @ sw1.T) * (xf @ sw3.T) @ sw2.T
        return (routed + shared).reshape(B, S, D)
    x = x + _L0_ffn_ref(_L0_cond_ref(x, itok_B_1_198, L0_cond_weights), L0_ffn_expert_bias, L0_ffn_gate_w, L0_ffn_w1, L0_ffn_w2, L0_ffn_w3, L0_ffn_sw1, L0_ffn_sw2, L0_ffn_sw3)
    return x

_drawn_inputs = setup_inputs


def setup_inputs(seed=0):
    import zlib

    import numpy as np

    out = dict(_drawn_inputs(seed))
    spreads = {'L0_ffn_expert_bias': (0.0, 0.8)}
    factors = {'L0_cond_weights': 4.216,
     'L0_ffn_gate_w': 8.0,
     'L0_ffn_w1': 8.0,
     'L0_ffn_w2': 8.0,
     'L0_ffn_w3': 8.0,
     'L0_ffn_sw1': 4.706,
     'L0_ffn_sw2': 4.603,
     'L0_ffn_sw3': 4.617}
    for name, (base, spread) in spreads.items():
        noise = np.random.default_rng([zlib.crc32(name.encode()), seed]).standard_normal(out[name].shape)
        drawn = base * np.exp(spread * noise) if base else spread * noise
        out[name] = jnp.asarray(drawn.astype(out[name].dtype))
    for name, factor in factors.items():
        out[name] = (out[name] * factor).astype(out[name].dtype)
    return out
```

```python
from contextlib import ExitStack

import concourse.bass as bass
from concourse import mybir

F32 = mybir.dt.float32
F32R = mybir.dt.float32r
I32 = mybir.dt.int32
U32 = mybir.dt.uint32
ALU = mybir.AluOpType
ACT = mybir.ActivationFunctionType
AX_X = mybir.AxisListType.X

P = 128
BATCH, CH, DIM = 32, 32, 256
KT = DIM // P
TOKENS = BATCH * CH
TILES = TOKENS // P
PER_TILE = P // CH
GROUPS = 2
GT = TOKENS // GROUPS
GTILES = TILES // GROUPS
EXPERTS = 8
HID = 128
W13 = KT * 2 * HID
WCOLS = W13 + DIM
STEPS = GROUPS * (EXPERTS + 1)
HBUFS = 4


def adaln_ffn_kernel(nc, x, index, cond_w, bias, gate, weights, residual, scratch, out):
    with ExitStack() as ctx:
        def sb(name, shape, dt=F32):
            return ctx.enter_context(nc.sbuf_tensor(name, shape, dt))

        def psum(name, shape):
            return ctx.enter_context(nc.psum_tensor(name, shape, F32))

        def sem(name):
            return ctx.enter_context(nc.semaphore(name))

        x_in = sb("x_in", [P, TILES, DIM])
        index_sb = sb("index_sb", [BATCH, 1], I32)
        cond_rows = sb("cond_rows", [BATCH, CH, CH])
        cond_turned = sb("cond_turned", [CH, CH, BATCH])
        cond_diag = sb("cond_diag", [P, TILES, P])
        gate_in = sb("gate_in", [P, KT, EXPERTS])
        gate_hi = sb("gate_hi", [P, KT, EXPERTS], F32R)
        gate_lo = sb("gate_lo", [P, KT, EXPERTS], F32R)
        bias_sb = sb("bias_sb", [P, EXPERTS])
        w_in = sb("w_in", [P, EXPERTS + 1, WCOLS])
        residual_sb = sb("residual_sb", [P, KT, TOKENS])
        xt_hi = sb("xt_hi", [P, KT, TOKENS], F32R)
        xt_lo = sb("xt_lo", [P, KT, TOKENS], F32R)
        w13_hi = [sb(f"w13_hi{i}", [P, W13], F32R) for i in range(2)]
        w13_lo = [sb(f"w13_lo{i}", [P, W13], F32R) for i in range(2)]
        w2_hi = [sb(f"w2_hi{i}", [P, DIM], F32R) for i in range(2)]
        w2_lo = [sb(f"w2_lo{i}", [P, DIM], F32R) for i in range(2)]
        identity = sb("identity", [P, P])
        earlier = sb("earlier", [P, EXPERTS, EXPERTS])
        score = sb("score", [P, TILES, EXPERTS])
        biased = sb("biased", [P, TILES, EXPERTS])
        above = sb("above", [P, TILES, EXPERTS, EXPERTS])
        tied = sb("tied", [P, TILES, EXPERTS, EXPERTS])
        rank = sb("rank", [P, TILES, EXPERTS])
        chosen = sb("chosen", [P, EXPERTS, TILES])
        chosen_t = sb("chosen_t", [EXPERTS * TILES, P])
        scale = sb("scale", [P, EXPERTS, TOKENS])
        sa = [sb(f"sa{i}", [P, GT]) for i in range(2)]
        sbb = [sb(f"sb{i}", [P, GT]) for i in range(2)]
        silu = [sb(f"silu{i}", [P, GT]) for i in range(2)]
        hidden = [sb(f"hidden{i}", [P, GT]) for i in range(2)]
        hid_hi = [sb(f"hid_hi{i}", [P, GT], F32R) for i in range(HBUFS)]
        hid_lo = [sb(f"hid_lo{i}", [P, GT], F32R) for i in range(HBUFS)]
        result = sb("result", [P, KT, TOKENS])
        warm = sb("warm", [P, 1])

        a_ps = [psum(f"a_ps{i}", [P, GT]) for i in range(2)]
        b_ps = [psum(f"b_ps{i}", [P, GT]) for i in range(2)]
        out_ps = [[psum(f"out_ps{m}{g}", [P, GT]) for g in range(GROUPS)] for m in range(KT)]
        score_ps = a_ps[1][:, 0:TILES * EXPERTS]
        chosen_ps = b_ps[1][0:EXPERTS * TILES, 0:P]

        index_loaded = sem("index_loaded")
        x_loaded = [sem(f"x_loaded{g}") for g in range(GROUPS)]
        gate_loaded = sem("gate_loaded")
        shared_loaded = sem("shared_loaded")
        routed_loaded = sem("routed_loaded")
        residual_loaded = sem("residual_loaded")
        cond_gathered = sem("cond_gathered")
        diag_zeroed = sem("diag_zeroed")
        cond_turned_ready = sem("cond_turned_ready")
        diag_ready = sem("diag_ready")
        identity_blank = sem("identity_blank")
        constants_ready = sem("constants_ready")
        mixed_ready = sem("mixed_ready")
        xt_hi_ready = sem("xt_hi_ready")
        xt_lo_ready = sem("xt_lo_ready")
        gate_hi_ready = sem("gate_hi_ready")
        gate_lo_ready = sem("gate_lo_ready")
        gate_done = sem("gate_done")
        score_ready = sem("score_ready")
        routing = sem("routing")
        chosen_ready = sem("chosen_ready")
        chosen_turned = sem("chosen_turned")
        chosen_t_ready = sem("chosen_t_ready")
        scale_written = sem("scale_written")
        scale_loaded = sem("scale_loaded")
        ab_ready = sem("ab_ready")
        ab_used = sem("ab_used")
        sa_ready = sem("sa_ready")
        sb_ready = sem("sb_ready")
        silu_ready = sem("silu_ready")
        hidden_ready = sem("hidden_ready")
        hid_hi_ready = sem("hid_hi_ready")
        hid_lo_ready = sem("hid_lo_ready")
        summed = sem("summed")
        w13_hi_ready = sem("w13_hi_ready")
        w13_lo_ready = sem("w13_lo_ready")
        w2_hi_ready = sem("w2_hi_ready")
        w2_lo_ready = sem("w2_lo_ready")
        result_ready = sem("result_ready")
        out_stored = sem("out_stored")

        block = ctx.enter_context(nc.Block())

        @block.sync
        def _(sp):
            sp.dma_start(index_sb[:], index).then_inc(index_loaded, 16)
            for g in range(GROUPS):
                sp.dma_start(x_in[:, g * GTILES:(g + 1) * GTILES, :],
                             x[:, g * GTILES:(g + 1) * GTILES, :]).then_inc(x_loaded[g], 16)
            sp.dma_start(gate_in[:], gate).then_inc(gate_loaded, 16)
            sp.dma_start(bias_sb[:], bias.partition_broadcast(P)).then_inc(gate_loaded, 16)
            sp.dma_start(w_in[:, 0, :], weights[:, 0, :]).then_inc(shared_loaded, 16)
            half = EXPERTS // 2
            for e in (1, 1 + half):
                sp.dma_start(w_in[:, e:e + half, :], weights[:, e:e + half, :]).then_inc(routed_loaded, 16)
            sp.wait_ge(chosen_t_ready, 1)
            sp.dma_start(scratch, chosen_t[:]).then_inc(scale_written, 16)
            sp.wait_ge(scale_written, 16)
            row = scratch.rearrange("r c -> (r c)")
            for e in (0, half):
                sp.dma_start(scale[:, e:e + half, :].rearrange("p e t -> p (e t)"),
                             row[e * TOKENS:(e + half) * TOKENS].partition_broadcast(P)).then_inc(scale_loaded, 16)
            sp.dma_start(residual_sb[:], residual).then_inc(residual_loaded, 16)
            for g in range(GROUPS):
                for m in range(KT):
                    sp.wait_ge(result_ready, g * KT + m + 1)
                    sp.dma_start(out[:, m, g * GT:(g + 1) * GT],
                                 result[:, m, g * GT:(g + 1) * GT]).then_inc(out_stored, 16)
            sp.wait_ge(out_stored, 16 * GROUPS * KT)

        @block.gpsimd
        def _(pool):
            pool.wait_ge(index_loaded, 16)
            pool.indirect_dma_start(
                out=cond_rows[:].rearrange("b c d -> b (c d)"), out_offset=None,
                in_=cond_w, in_offset=bass.IndirectOffsetOnAxis(ap=index_sb[:].bitcast(U32), axis=0),
            ).then_inc(cond_gathered, 16)
            pool.memset(identity[:], 0.0).then_inc(identity_blank, 1)
            pool.memset(earlier[:], 1.0).then_inc(identity_blank, 1)
            pool.wait_ge(identity_blank, 2)
            pool.affine_select(out=identity[:], in_=identity[:], compare_op=ALU.not_equal, fill=1.0,
                               base=0, pattern=[[-1, P]], channel_multiplier=1).then_inc(constants_ready, 1)
            pool.affine_select(out=earlier[:], in_=earlier[:], compare_op=ALU.is_gt, fill=0.0,
                               base=0, pattern=[[1, EXPERTS], [-1, EXPERTS]],
                               channel_multiplier=0).then_inc(constants_ready, 1)

            def w13_low(e, slot, source):
                pool.wait_ge(w13_hi_ready, e + 1)
                pool.tensor_tensor(w13_lo[slot][:], w_in[:, source, 0:W13], w13_hi[slot][:].bitcast(F32),
                                   ALU.subtract).then_inc(w13_lo_ready, 1)

            def w2_low(e, slot, source):
                pool.wait_ge(w2_hi_ready, e + 1)
                pool.tensor_tensor(w2_lo[slot][:], w_in[:, source, W13:WCOLS], w2_hi[slot][:].bitcast(F32),
                                   ALU.subtract).then_inc(w2_lo_ready, 1)

            w13_low(0, 0, 0)
            w13_low(1, 1, 1)
            w2_low(0, 0, 0)
            with pool.Fori(0, EXPERTS // 2 - 1) as i:
                for k in (1, 2):
                    e = i * 2 + k
                    w13_low(e + 1, (k + 1) % 2, bass.ds(e + 1, 1))
                    w2_low(e, k % 2, bass.ds(e, 1))
            w13_low(EXPERTS, 0, EXPERTS)
            w2_low(EXPERTS - 1, 1, EXPERTS - 1)
            w2_low(EXPERTS, 0, EXPERTS)

        @block.scalar
        def _(act):
            def w13_high(e, slot, source, reuse=True):
                if reuse:
                    act.wait_ge(ab_ready, (e - 2) * 4 + 4)
                act.copy(w13_hi[slot][:], w_in[:, source, 0:W13]).then_inc(w13_hi_ready, 1)

            def w2_high(e, slot, source, reuse=True):
                if reuse:
                    act.wait_ge(summed, (e - 2) * 4 + 4)
                act.copy(w2_hi[slot][:], w_in[:, source, W13:WCOLS]).then_inc(w2_hi_ready, 1)

            def silu_step(n, k, reuse=True):
                act.wait_ge(sa_ready, n - 1)
                act.wait_ge(hidden_ready, n - 1)
                act.activation(silu[k % 2][:], sa[k % 2][:], ACT.Silu).then_inc(silu_ready, 1)

            def high_step(n, k, reuse=True):
                act.wait_ge(hidden_ready, n + 1)
                if reuse:
                    act.wait_ge(summed, (n - HBUFS) * 2 + 2)
                act.copy(hid_hi[k % HBUFS][:], hidden[k % 2][:]).then_inc(hid_hi_ready, 1)

            act.wait_ge(gate_loaded, 32)
            act.copy(gate_hi[:], gate_in[:]).then_inc(gate_hi_ready, 1)
            act.wait_ge(shared_loaded, 16)
            w13_high(0, 0, 0, reuse=False)
            for g in range(GROUPS):
                act.wait_ge(mixed_ready, g + 1)
                for m in range(KT):
                    act.copy(xt_hi[:, m, g * GT:(g + 1) * GT], out_ps[m][g][:]).then_inc(xt_hi_ready, 1)
            act.wait_ge(gate_done, 1)
            act.activation(score[:].rearrange("p t e -> p (t e)"), score_ps, ACT.Sigmoid).then_inc(score_ready, 1)
            for n in range(GROUPS):
                act.wait_ge(ab_ready, 2 * n + 1)
                act.activation(silu[n][:], a_ps[n][:], ACT.Silu).then_inc(silu_ready, 1)
                if n == 0:
                    act.wait_ge(routed_loaded, 32)
                    w13_high(1, 1, 1, reuse=False)
                else:
                    w2_high(0, 0, 0, reuse=False)
                high_step(n, n, reuse=False)
            act.wait_ge(chosen_turned, 1)
            act.copy(chosen_t[:], chosen_ps).then_inc(chosen_t_ready, 1)

            def expert(e, k, source13, source2, last=False):
                n = e * 2
                silu_step(n, 2 * k)
                if not last:
                    w13_high(e + 1, (k + 1) % 2, source13)
                high_step(n, 2 * k)
                silu_step(n + 1, 2 * k + 1)
                w2_high(e, k % 2, source2)
                high_step(n + 1, 2 * k + 1)

            silu_step(2, 2)
            w13_high(2, 0, 2)
            high_step(2, 2, reuse=False)
            silu_step(3, 3)
            w2_high(1, 1, 1, reuse=False)
            high_step(3, 3, reuse=False)
            with act.Fori(0, EXPERTS // 2 - 1) as i:
                for k in (2, 3):
                    e = i * 2 + k
                    expert(e, k, bass.ds(e + 1, 1), bass.ds(e, 1))
            expert(EXPERTS, EXPERTS, None, EXPERTS, last=True)

        @block.vector
        def _(dve):
            dve.memset(cond_diag[:], 0.0).then_inc(diag_zeroed, 1)
            dve.wait_ge(cond_gathered, 16)
            dve.transpose(cond_turned[:], cond_rows[:].rearrange("b c d -> b d c")).then_inc(cond_turned_ready, 1)
            dve.wait_ge(cond_turned_ready, 1)
            dve.wait_ge(diag_zeroed, 1)
            for j in range(PER_TILE):
                dve.tensor_copy(cond_diag[j * CH:(j + 1) * CH, :, j * CH:(j + 1) * CH],
                                cond_turned[:].rearrange("c d (i j) -> c i d j", j=PER_TILE)[:, :, :, j]
                                ).then_inc(diag_ready, 1)
            dve.wait_ge(gate_hi_ready, 1)
            dve.tensor_tensor(gate_lo[:], gate_in[:], gate_hi[:].bitcast(F32), ALU.subtract).then_inc(gate_lo_ready, 1)
            for g in range(GROUPS):
                for m in range(KT):
                    dve.wait_ge(xt_hi_ready, g * KT + m + 1)
                    dve.tensor_tensor(xt_lo[:, m, g * GT:(g + 1) * GT], out_ps[m][g][:],
                                      xt_hi[:, m, g * GT:(g + 1) * GT].bitcast(F32),
                                      ALU.subtract).then_inc(xt_lo_ready, 1)

            def low_step(n, k):
                dve.wait_ge(hid_hi_ready, n + 1)
                dve.tensor_tensor(hid_lo[k % HBUFS][:], hidden[k % 2][:], hid_hi[k % HBUFS][:].bitcast(F32),
                                  ALU.subtract).then_inc(hid_lo_ready, 1)

            dve.wait_ge(score_ready, 1)
            dve.tensor_tensor(biased[:], score[:],
                              bias_sb[:].rearrange("p (o e) -> p o e", o=1).to_broadcast([P, TILES, EXPERTS]),
                              ALU.add).then_inc(routing, 1)
            dve.wait_ge(routing, 1)
            other = biased[:].rearrange("p t (o e) -> p t o e", o=1).to_broadcast([P, TILES, EXPERTS, EXPERTS])
            own = biased[:].rearrange("p t (e o) -> p t e o", o=1).to_broadcast([P, TILES, EXPERTS, EXPERTS])
            dve.tensor_tensor(above[:], other, own, ALU.is_gt).then_inc(routing, 1)
            dve.tensor_tensor(tied[:], other, own, ALU.is_equal).then_inc(routing, 1)
            dve.wait_ge(constants_ready, 2)
            dve.wait_ge(routing, 3)
            dve.tensor_tensor(tied[:], tied[:],
                              earlier[:].rearrange("p (o e) f -> p o e f", o=1)
                              .to_broadcast([P, TILES, EXPERTS, EXPERTS]), ALU.mult).then_inc(routing, 1)
            dve.wait_ge(routing, 4)
            dve.tensor_tensor(above[:], above[:], tied[:], ALU.add).then_inc(routing, 1)
            dve.wait_ge(routing, 5)
            dve.tensor_reduce(rank[:], above[:], AX_X, ALU.add).then_inc(routing, 1)
            dve.wait_ge(routing, 6)
            dve.scalar_tensor_tensor(out=chosen[:].rearrange("p e t -> p t e"), in0=rank[:], scalar=2.0,
                                     in1=score[:], op0=ALU.is_lt, op1=ALU.mult).then_inc(chosen_ready, 1)

            for n in range(GROUPS):
                dve.wait_ge(ab_ready, 2 * n + 2)
                dve.wait_ge(silu_ready, n + 1)
                dve.tensor_tensor(hidden[n][:], silu[n][:], b_ps[n][:], ALU.mult).then_inc(hidden_ready, 1)
                low_step(n, n)

            def step(n, k, e, first=False):
                g = k % 2
                span = scale[:, e, g * GT:(g + 1) * GT]
                if len(span.shape) == 3:
                    span = span.rearrange("p o t -> p (o t)")
                dve.wait_ge(ab_ready, n * 2 + 1)
                dve.wait_ge(silu_ready, n - 1)
                dve.tensor_tensor(sa[k % 2][:], a_ps[k % 2][:], span, ALU.mult).then_inc(sa_ready, 1)
                dve.wait_ge(ab_ready, n * 2 + 2)
                dve.tensor_tensor(sbb[k % 2][:], b_ps[k % 2][:], span, ALU.mult).then_inc(sb_ready, 1)
                if not first:
                    low_step(n - 1, k - 1)
                dve.wait_ge(silu_ready, n + 1)
                dve.wait_ge(sb_ready, n - 1)
                dve.wait_ge(hid_hi_ready, n - 1)
                dve.tensor_tensor(hidden[k % 2][:], silu[k % 2][:], sbb[k % 2][:],
                                  ALU.mult).then_inc(hidden_ready, 1)

            dve.wait_ge(scale_loaded, 32)
            step(2, 2, 0, first=True)
            step(3, 3, 0)
            with dve.Fori(0, EXPERTS // 2 - 1) as i:
                for k in range(4, 8):
                    step(i * 4 + k, k, bass.ds(i * 2 + (k // 2 - 1), 1))
            for n in (STEPS - 2, STEPS - 1):
                step(n, n, EXPERTS - 1)
            low_step(STEPS - 1, STEPS - 1)
            dve.wait_ge(residual_loaded, 16)
            for g in range(GROUPS):
                for m in range(KT):
                    dve.wait_ge(summed, 2 * (STEPS - 2 + g) + m + 1)
                    dve.tensor_tensor(result[:, m, g * GT:(g + 1) * GT], out_ps[m][g][:],
                                      residual_sb[:, m, g * GT:(g + 1) * GT], ALU.add).then_inc(result_ready, 1)

        @block.tensor
        def _(pe):
            pe.wait_ge(diag_ready, PER_TILE)
            for g in range(GROUPS):
                pe.wait_ge(x_loaded[g], 16)
                for t in range(g * GTILES, (g + 1) * GTILES):
                    for m in range(KT):
                        col = (t - g * GTILES) * P
                        last = pe.matmul(out_ps[m][g][:, col:col + P], x_in[:, t, m * P:(m + 1) * P],
                                         cond_diag[:, t, :], start=True, stop=True)
                last.then_inc(mixed_ready, 1)
            pe.wait_ge(gate_lo_ready, 1)
            for g in range(GROUPS):
                pe.wait_ge(xt_hi_ready, KT * (g + 1))
                pe.wait_ge(xt_lo_ready, KT * (g + 1))
                for t in range(g * GTILES, (g + 1) * GTILES):
                    passes = [(xv, gv, m) for m in range(KT)
                              for xv, gv in ((xt_hi, gate_hi), (xt_hi, gate_lo), (xt_lo, gate_hi))]
                    for i, (xv, gv, m) in enumerate(passes):
                        last = pe.matmul(score_ps[:, t * EXPERTS:(t + 1) * EXPERTS], xv[:, m, t * P:(t + 1) * P],
                                         gv[:, m, :], start=(i == 0), stop=(i == len(passes) - 1))
            last.then_inc(gate_done, 1)

            def up_step(n, k, e, slot):
                g = k % 2
                if k >= 2:
                    pe.wait_ge(hidden_ready if k < 4 else sb_ready, n - 1 if k < 4 else n - 3)
                if g == 0:
                    pe.wait_ge(w13_hi_ready, e + 1)
                    pe.wait_ge(w13_lo_ready, e + 1)
                for which, bank in enumerate((a_ps[k % 2], b_ps[k % 2])):
                    for m in range(KT):
                        col = (m * 2 + which) * HID
                        for i, (wv, xv) in enumerate(((w13_hi[slot], xt_hi), (w13_hi[slot], xt_lo), (w13_lo[slot], xt_hi))):
                            last = pe.matmul(bank[:], wv[:, col:col + HID], xv[:, m, g * GT:(g + 1) * GT],
                                             start=(m == 0 and i == 0), stop=(m == KT - 1 and i == 2))
                    last.then_inc(ab_ready, 1)

            def down_step(n, k, e, slot, first=False, final=False):
                g = k % 2
                if g == 0:
                    pe.wait_ge(w2_hi_ready, e + 1)
                    pe.wait_ge(w2_lo_ready, e + 1)
                pe.wait_ge(hid_hi_ready, n + 1)
                for m in range(KT):
                    for i, (wv, hv) in enumerate(((w2_hi, hid_hi), (w2_lo, hid_hi), (w2_hi, hid_lo))):
                        if m == 0 and i == 2:
                            pe.wait_ge(hid_lo_ready, n + 1)
                        last = pe.matmul(out_ps[m][g][:], wv[slot][:, m * P:(m + 1) * P], hv[k % HBUFS][:],
                                         start=first and i == 0, stop=final and i == 2, skip_group_check=True)
                    last.then_inc(summed, 1)

            up_step(0, 0, 0, 0)
            pe.wait_ge(score_ready, 1)
            up_step(1, 1, 0, 0)
            pe.wait_ge(hidden_ready, 2)
            pe.wait_ge(chosen_ready, 1)
            pe.wait_ge(constants_ready, 2)
            pe.transpose(chosen_ps, chosen[:].rearrange("p e t -> p (e t)"), identity[:]).then_inc(chosen_turned, 1)
            up_step(2, 2, 1, 1)
            down_step(0, 0, 0, 0, first=True)
            pe.wait_ge(chosen_t_ready, 1)
            up_step(3, 3, 1, 1)
            down_step(1, 1, 0, 0, first=True)
            with pe.Fori(0, EXPERTS // 2 - 1) as i:
                for k in range(4, 8):
                    up_step(i * 4 + k, k, i * 2 + k // 2, (k // 2) % 2)
                    down_step(i * 4 + (k - 2), k - 2, i * 2 + (k // 2 - 1), (k // 2 - 1) % 2)
            for n in (STEPS - 2, STEPS - 1):
                up_step(n, n, EXPERTS, 0)
                down_step(n - 2, n - 2, EXPERTS - 1, 1)
            for n in (STEPS - 2, STEPS - 1):
                down_step(n, n, EXPERTS, 0, final=True)


def kernel(x, itok_B_1_198, L0_cond_weights, L0_ffn_expert_bias, L0_ffn_gate_w, L0_ffn_w1, L0_ffn_w2, L0_ffn_w3,
           L0_ffn_sw1, L0_ffn_sw2, L0_ffn_sw3):
    import numpy as np
    import concourse.bacc as bacc
    from concourse.bass_utils import run_bass_kernel_spmd

    x = np.asarray(x)
    x_tiles = x.reshape(TILES, P, DIM).transpose(1, 0, 2)
    residual = x.reshape(TOKENS, KT, P).transpose(2, 1, 0)

    def turned(w, sw):
        return np.concatenate([np.asarray(sw)[None], np.asarray(w)]).transpose(2, 0, 1)

    def halves(w):
        return w.reshape(KT, P, EXPERTS + 1, 1, HID).transpose(1, 2, 0, 3, 4)

    w13 = np.concatenate([halves(turned(L0_ffn_w1, L0_ffn_sw1)), halves(turned(L0_ffn_w3, L0_ffn_sw3))], axis=3)
    w2 = turned(L0_ffn_w2, L0_ffn_sw2)
    weights = np.concatenate([w13.reshape(P, EXPERTS + 1, W13), w2], axis=2)
    gate = np.asarray(L0_ffn_gate_w).T.reshape(KT, P, EXPERTS).transpose(1, 0, 2)
    arrays = {
        "x": x_tiles,
        "index": np.asarray(itok_B_1_198).reshape(BATCH, 1),
        "cond_w": np.asarray(L0_cond_weights).reshape(-1, CH * CH),
        "bias": np.asarray(L0_ffn_expert_bias),
        "gate": gate,
        "weights": weights,
        "residual": residual,
    }
    arrays = {name: np.ascontiguousarray(a) for name, a in arrays.items()}
    nc = bacc.Bacc("TRN2", target_bir_lowering=False, num_devices=1)
    args = [nc.dram_tensor(name, a.shape, mybir.dt.from_np(a.dtype), kind="ExternalInput").ap()
            for name, a in arrays.items()]
    scratch = nc.dram_tensor("scratch", (EXPERTS * TILES, P), F32, kind="Internal").ap()
    out = nc.dram_tensor("out", (P, KT, TOKENS), F32, kind="ExternalOutput").ap()
    adaln_ffn_kernel(nc, *args, scratch, out)
    got = run_bass_kernel_spmd(nc, [arrays], core_ids=[0]).results[0]["out"]
    return got.transpose(2, 1, 0).reshape(BATCH, CH, DIM)
```

```python
from contextlib import ExitStack

import concourse.bass as bass
from concourse import mybir

F32 = mybir.dt.float32
F32R = mybir.dt.float32r
BF16 = mybir.dt.bfloat16
I32 = mybir.dt.int32
U32 = mybir.dt.uint32
ALU = mybir.AluOpType
ACT = mybir.ActivationFunctionType
AX_X = mybir.AxisListType.X

P = 128
BATCH, CH, DIM = 32, 32, 256
KT = DIM // P
TOKENS = BATCH * CH
TILES = TOKENS // P
PER_TILE = P // CH
GROUPS = 2
GT = TOKENS // GROUPS
GTILES = TILES // GROUPS
EXPERTS = 8
HID = 128
W13 = KT * 2 * HID
WCOLS = W13 + DIM
PAIRS = EXPERTS // 2
HBUFS = 4
WARM_UP = 20


def adaln_ffn_kernel(nc, x, index, cond_w, bias, gate, weights, residual, scratch, out):
    with ExitStack() as ctx:
        def sb(name, shape, dt=F32):
            return ctx.enter_context(nc.sbuf_tensor(name, shape, dt))

        def psum(name, shape):
            return ctx.enter_context(nc.psum_tensor(name, shape, F32))

        def sem(name):
            return ctx.enter_context(nc.semaphore(name))

        x_in = sb("x_in", [P, TILES, DIM])
        index_sb = sb("index_sb", [BATCH, 1], I32)
        cond_rows = sb("cond_rows", [BATCH, CH, CH])
        cond_turned = sb("cond_turned", [CH, CH, BATCH])
        cond_diag = sb("cond_diag", [P, TILES, P])
        gate_in = sb("gate_in", [P, KT, EXPERTS])
        gate_hi = sb("gate_hi", [P, KT, P], F32R)
        gate_lo = sb("gate_lo", [P, KT, P], F32R)
        logit_t = sb("logit_t", [EXPERTS, TOKENS])
        bias_sb = sb("bias_sb", [P, EXPERTS])
        w_in = sb("w_in", [P, EXPERTS + 1, WCOLS])
        residual_sb = sb("residual_sb", [P, KT, TOKENS])
        xt_hi = sb("xt_hi", [P, KT, TOKENS], F32R)
        xt_lo = sb("xt_lo", [P, KT, TOKENS], F32R)
        w13_hi = [sb(f"w13_hi{i}", [P, W13], F32R) for i in range(2)]
        w13_lo = [sb(f"w13_lo{i}", [P, W13], F32R) for i in range(2)]
        w2_hi = [sb(f"w2_hi{i}", [P, DIM], F32R) for i in range(2)]
        w2_lo = [sb(f"w2_lo{i}", [P, DIM], F32R) for i in range(2)]
        identity = sb("identity", [P, P])
        score = sb("score", [P, TILES, EXPERTS])
        biased = sb("biased", [P, TILES, EXPERTS])
        top = sb("top", [P, TILES, 8])
        within = sb("within", [P, TILES, EXPERTS])
        second = sb("second", [P, TILES, EXPERTS])
        second_count = sb("second_count", [P, TILES, EXPERTS])
        both = sb("both", [P, TILES])
        served = sb("served", [P, TILES, EXPERTS])
        eights = sb("eights", [P, 1])
        falling_i = sb("falling_i", [1, EXPERTS], I32)
        falling = sb("falling", [1, EXPERTS])
        count8 = sb("count8", [1, EXPERTS])
        key = sb("key", [1, EXPERTS])
        key_sorted = sb("key_sorted", [1, EXPERTS])
        used = sb("used", [1, EXPERTS])
        unkeyed = sb("unkeyed", [1, EXPERTS])
        order = sb("order", [1, 2 * EXPERTS], I32)
        pairs = sb("pairs", [1, 1], I32)
        chosen = sb("chosen", [P, EXPERTS, TILES])
        chosen_t = sb("chosen_t", [EXPERTS * TILES, P])
        scale = sb("scale", [P, EXPERTS, TOKENS])
        sa = [sb(f"sa{i}", [P, GT]) for i in range(2)]
        sbb = [sb(f"sb{i}", [P, GT]) for i in range(2)]
        silu = [sb(f"silu{i}", [P, GT]) for i in range(2)]
        hidden = [sb(f"hidden{i}", [P, GT]) for i in range(2)]
        hid_hi = [sb(f"hid_hi{i}", [P, GT], F32R) for i in range(HBUFS)]
        hid_lo = [sb(f"hid_lo{i}", [P, GT], F32R) for i in range(HBUFS)]
        result = sb("result", [P, KT, TOKENS])
        warm = sb("warm", [P, GT], BF16)

        a_ps = [psum(f"a_ps{i}", [P, GT]) for i in range(2)]
        b_ps = [psum(f"b_ps{i}", [P, GT]) for i in range(2)]
        out_ps = [[psum(f"out_ps{m}{g}", [P, GT]) for g in range(GROUPS)] for m in range(KT)]
        logit_ps = (a_ps[1], b_ps[1])
        score_ps = a_ps[1][:, 0:TILES * EXPERTS]
        chosen_ps = b_ps[1][0:EXPERTS * TILES, 0:P]
        count_ps = a_ps[1][0:1, P:P + TILES * EXPERTS]

        index_loaded = sem("index_loaded")
        x_loaded = [sem(f"x_loaded{g}") for g in range(GROUPS)]
        gate_loaded = sem("gate_loaded")
        shared_loaded = sem("shared_loaded")
        routed_loaded = sem("routed_loaded")
        residual_loaded = sem("residual_loaded")
        gather_started = sem("gather_started")
        cond_gathered = sem("cond_gathered")
        warm_zeroed = sem("warm_zeroed")
        diag_zeroed = sem("diag_zeroed")
        cond_turned_ready = sem("cond_turned_ready")
        diag_ready = sem("diag_ready")
        constants_blank = sem("constants_blank")
        constants_ready = sem("constants_ready")
        mixed_ready = sem("mixed_ready")
        xt_hi_ready = sem("xt_hi_ready")
        xt_lo_ready = sem("xt_lo_ready")
        gate_hi_ready = sem("gate_hi_ready")
        gate_lo_ready = sem("gate_lo_ready")
        logit_done = sem("logit_done")
        logit_t_ready = sem("logit_t_ready")
        logit_turned = sem("logit_turned")
        score_ready = sem("score_ready")
        routing = sem("routing")
        served_ready = sem("served_ready")
        chosen_ready = sem("chosen_ready")
        chosen_turned = sem("chosen_turned")
        counted = sem("counted")
        ordering = sem("ordering")
        order_ready = sem("order_ready")
        chosen_t_ready = sem("chosen_t_ready")
        scale_written = sem("scale_written")
        scale_loaded = sem("scale_loaded")
        ab_ready = sem("ab_ready")
        sa_ready = sem("sa_ready")
        sb_ready = sem("sb_ready")
        silu_ready = sem("silu_ready")
        hidden_ready = sem("hidden_ready")
        hid_hi_ready = sem("hid_hi_ready")
        hid_lo_ready = sem("hid_lo_ready")
        summed = sem("summed")
        w13_hi_ready = sem("w13_hi_ready")
        w13_lo_ready = sem("w13_lo_ready")
        w2_hi_ready = sem("w2_hi_ready")
        w2_lo_ready = sem("w2_lo_ready")
        result_ready = sem("result_ready")
        out_stored = sem("out_stored")

        block = ctx.enter_context(nc.Block())

        def pairs_to_run(engine):
            engine.wait_ge(order_ready, 2)
            return engine.value_load(pairs[0:1, 0:1], min_val=1, max_val=PAIRS)

        def expert_of(engine, turn):
            at = turn - 1
            cell = order[0:1, at:at + 1] if isinstance(at, int) else order[0:1, bass.ds(at, 1)]
            return engine.value_load(cell, min_val=0, max_val=EXPERTS - 1)

        @block.sync
        def _(sp):
            sp.dma_start(index_sb[:], index).then_inc(index_loaded, 16)
            sp.dma_start(x_in[:, 0:GTILES, :], x[:, 0:GTILES, :]).then_inc(x_loaded[0], 16)
            sp.wait_ge(gather_started, 1)
            sp.dma_start(x_in[:, GTILES:TILES, :], x[:, GTILES:TILES, :]).then_inc(x_loaded[1], 16)
            sp.dma_start(gate_in[:], gate).then_inc(gate_loaded, 16)
            sp.dma_start(bias_sb[:], bias.partition_broadcast(P)).then_inc(gate_loaded, 16)
            sp.dma_start(w_in[:, 0, :], weights[:, 0, :]).then_inc(shared_loaded, 16)
            for e in (1, 1 + PAIRS):
                sp.dma_start(w_in[:, e:e + PAIRS, :], weights[:, e:e + PAIRS, :]).then_inc(routed_loaded, 16)
            sp.dma_start(residual_sb[:], residual).then_inc(residual_loaded, 16)
            sp.wait_ge(chosen_t_ready, 1)
            sp.dma_start(scratch, chosen_t[:]).then_inc(scale_written, 16)

            rows = scratch.rearrange("(e t) c -> e (t c)", e=EXPERTS)

            def load_scale(turn, cell):
                e = expert_of(sp, turn)
                sp.dma_start(scale[:, cell, :], rows[bass.ds(e, 1), :].to_broadcast([P, TOKENS])).then_inc(scale_loaded, 16)

            running = pairs_to_run(sp)
            sp.wait_ge(scale_written, 16)
            for turn in (1, 2):
                load_scale(turn, turn - 1)
            with sp.Fori(1, PAIRS) as i:
                with sp.If(running > i):
                    sp.wait_ge(scale_loaded, i * 32)
                    for k in (1, 2):
                        load_scale(i * 2 + k, bass.ds(i * 2 + (k - 1), 1))
            for g in range(GROUPS):
                for m in range(KT):
                    sp.wait_ge(result_ready, g * KT + m + 1)
                    sp.dma_start(out[:, m, g * GT:(g + 1) * GT],
                                 result[:, m, g * GT:(g + 1) * GT]).then_inc(out_stored, 16)
            sp.wait_ge(out_stored, 16 * GROUPS * KT)

        @block.gpsimd
        def _(pool):
            pool.wait_ge(index_loaded, 16)
            pool.indirect_dma_start(
                out=cond_rows[:].rearrange("b c d -> b (c d)"), out_offset=None,
                in_=cond_w, in_offset=bass.IndirectOffsetOnAxis(ap=index_sb[:].bitcast(U32), axis=0),
                engine_sem=gather_started,
            ).then_inc(cond_gathered, 16)
            pool.memset(identity[:], 0.0).then_inc(constants_blank, 1)
            pool.memset(within[:], 1.0).then_inc(constants_blank, 1)
            pool.memset(eights[:], 8.0).then_inc(constants_ready, 1)
            pool.memset(order[:], 0).then_inc(constants_ready, 1)
            pool.iota(falling_i[:], pattern=[[-1, EXPERTS]], base=EXPERTS - 1,
                      channel_multiplier=0).then_inc(constants_ready, 1)
            pool.wait_ge(constants_blank, 2)
            pool.affine_select(out=identity[:], in_=identity[:], compare_op=ALU.not_equal, fill=1.0,
                               base=0, pattern=[[-1, P]], channel_multiplier=1).then_inc(constants_ready, 1)
            pool.memset(within[:, :, 0:1], 0.0).then_inc(constants_ready, 1)

            def w13_low(turn, slot, source):
                pool.wait_ge(w13_hi_ready, turn + 1)
                pool.tensor_tensor(w13_lo[slot][:], w_in[:, source, 0:W13], w13_hi[slot][:].bitcast(F32),
                                   ALU.subtract).then_inc(w13_lo_ready, 1)

            def w2_low(turn, slot, source):
                pool.wait_ge(w2_hi_ready, turn + 1)
                pool.tensor_tensor(w2_lo[slot][:], w_in[:, source, W13:WCOLS], w2_hi[slot][:].bitcast(F32),
                                   ALU.subtract).then_inc(w2_lo_ready, 1)

            def pair(turn):
                first, then, next_ = (expert_of(pool, turn + k) for k in range(3))
                w13_low(turn + 1, 0, bass.ds(then + 1, 1))
                w2_low(turn, 1, bass.ds(first + 1, 1))
                w13_low(turn + 2, 1, bass.ds(next_ + 1, 1))
                w2_low(turn + 1, 0, bass.ds(then + 1, 1))

            w13_low(0, 0, 0)
            w2_low(0, 0, 0)
            running = pairs_to_run(pool)
            w13_low(1, 1, bass.ds(expert_of(pool, 1) + 1, 1))
            pair(1)
            with pool.Fori(1, PAIRS) as i:
                with pool.If(running > i):
                    pair(i * 2 + 1)

        @block.scalar
        def _(act):
            def w13_high(slot, source):
                act.copy(w13_hi[slot][:], w_in[:, source, 0:W13]).then_inc(w13_hi_ready, 1)

            def w2_high(slot, source):
                act.copy(w2_hi[slot][:], w_in[:, source, W13:WCOLS]).then_inc(w2_hi_ready, 1)

            def silu_step(n, k):
                act.wait_ge(sa_ready, n - 1)
                act.wait_ge(hidden_ready, n - 1)
                act.activation(silu[k % 2][:], sa[k % 2][:], ACT.Silu).then_inc(silu_ready, 1)

            def high_step(n, k):
                act.wait_ge(hidden_ready, n + 1)
                act.copy(hid_hi[k % HBUFS][:], hidden[k % 2][:]).then_inc(hid_hi_ready, 1)

            act.wait_ge(gate_loaded, 32)
            act.wait_ge(gate_hi_ready, 1)
            act.copy(gate_hi[:, :, 0:EXPERTS], gate_in[:]).then_inc(gate_hi_ready, 1)
            act.wait_ge(shared_loaded, 16)
            w13_high(0, 0)
            w2_high(0, 0)
            for g in range(GROUPS):
                act.wait_ge(mixed_ready, g + 1)
                for m in range(KT):
                    act.copy(xt_hi[:, m, g * GT:(g + 1) * GT], out_ps[m][g][:]).then_inc(xt_hi_ready, 1)
            for g in range(GROUPS):
                act.wait_ge(logit_done, g + 1)
                act.copy(logit_t[:, g * GT:(g + 1) * GT], logit_ps[g][0:EXPERTS, :]).then_inc(logit_t_ready, 1)
            act.wait_ge(logit_turned, 1)
            act.activation(score[:].rearrange("p t e -> p (t e)"), score_ps, ACT.Sigmoid).then_inc(score_ready, 1)
            act.wait_ge(ab_ready, 1)
            act.activation(silu[0][:], a_ps[0][:], ACT.Silu).then_inc(silu_ready, 1)
            act.wait_ge(chosen_turned, 1)
            act.copy(chosen_t[:], chosen_ps).then_inc(chosen_t_ready, 1)
            high_step(0, 0)
            running = pairs_to_run(act)
            act.wait_ge(routed_loaded, 32)
            w13_high(1, bass.ds(expert_of(act, 1) + 1, 1))
            act.wait_ge(ab_ready, 3)
            act.activation(silu[1][:], a_ps[1][:], ACT.Silu).then_inc(silu_ready, 1)
            high_step(1, 1)

            def pair(turn):
                first, then, next_ = (expert_of(act, turn + k) for k in range(3))
                n = turn * 2
                silu_step(n, 2)
                w13_high(0, bass.ds(then + 1, 1))
                high_step(n, 2)
                silu_step(n + 1, 3)
                w2_high(1, bass.ds(first + 1, 1))
                high_step(n + 1, 3)
                silu_step(n + 2, 4)
                w13_high(1, bass.ds(next_ + 1, 1))
                high_step(n + 2, 4)
                silu_step(n + 3, 5)
                w2_high(0, bass.ds(then + 1, 1))
                high_step(n + 3, 5)

            pair(1)
            with act.Fori(1, PAIRS) as i:
                with act.If(running > i):
                    pair(i * 2 + 1)

        @block.vector
        def _(dve):
            dve.memset(warm[:], 0.0).then_inc(warm_zeroed, 1)
            dve.memset(cond_diag[:], 0.0).then_inc(diag_zeroed, 1)
            dve.memset(gate_hi[:].bitcast(F32), 0.0).then_inc(gate_hi_ready, 1)
            dve.memset(gate_lo[:].bitcast(F32), 0.0).then_inc(gate_lo_ready, 1)
            dve.wait_ge(cond_gathered, 16)
            dve.transpose(cond_turned[:], cond_rows[:].rearrange("b c d -> b d c")).then_inc(cond_turned_ready, 1)
            dve.wait_ge(cond_turned_ready, 1)
            dve.wait_ge(diag_zeroed, 1)
            turned = cond_turned[:].rearrange("c d (i j) -> c i d j", j=PER_TILE)
            for g in range(GROUPS):
                tiles = slice(g * GTILES, (g + 1) * GTILES)
                for j in range(PER_TILE):
                    dve.tensor_copy(cond_diag[j * CH:(j + 1) * CH, tiles, j * CH:(j + 1) * CH],
                                    turned[:, tiles, :, j]).then_inc(diag_ready, 1)
            dve.wait_ge(gate_hi_ready, 2)
            dve.wait_ge(gate_lo_ready, 1)
            dve.tensor_tensor(gate_lo[:, :, 0:EXPERTS], gate_in[:], gate_hi[:, :, 0:EXPERTS].bitcast(F32),
                              ALU.subtract).then_inc(gate_lo_ready, 1)
            dve.wait_ge(constants_ready, 5)
            dve.tensor_copy(falling[:], falling_i[:]).then_inc(ordering, 1)
            for g in range(GROUPS):
                for m in range(KT):
                    dve.wait_ge(xt_hi_ready, g * KT + m + 1)
                    dve.tensor_tensor(xt_lo[:, m, g * GT:(g + 1) * GT], out_ps[m][g][:],
                                      xt_hi[:, m, g * GT:(g + 1) * GT].bitcast(F32),
                                      ALU.subtract).then_inc(xt_lo_ready, 1)

            steps = [0]

            def then(instruction, done=None):
                steps[0] += 1
                instruction.then_inc(routing, 1)
                dve.wait_ge(routing, steps[0])

            grid = [P, TILES, EXPERTS]
            highest, runner = top[:, :, 0:1], top[:, :, 1:2]
            dve.wait_ge(score_ready, 1)
            then(dve.tensor_tensor(biased[:], score[:],
                                   bias_sb[:].rearrange("p (o e) -> p o e", o=1).to_broadcast(grid), ALU.add))
            for t in range(TILES):
                last = dve.max(top[:, t, :], biased[:, t, :])
            then(last)
            dve.tensor_tensor(second[:], biased[:], runner.to_broadcast(grid), ALU.is_equal).then_inc(routing, 1)
            dve.tensor_tensor(both[:].rearrange("p (t o) -> p t o", o=1), highest, runner,
                              ALU.is_equal).then_inc(routing, 1)
            dve.tensor_tensor(served[:], biased[:], runner.to_broadcast(grid), ALU.is_gt).then_inc(routing, 1)
            steps[0] += 3
            dve.wait_ge(routing, steps[0])
            then(dve.tensor_tensor_scan(second_count[:].rearrange("p t e -> p (t e)"),
                                        within[:].rearrange("p t e -> p (t e)"),
                                        second[:].rearrange("p t e -> p (t e)"), 0.0, ALU.mult, ALU.add))
            then(dve.scalar_tensor_tensor(out=second_count[:], in0=second_count[:], scalar=-1.0,
                                          in1=both[:].rearrange("p (t o) -> p t o", o=1).to_broadcast(grid),
                                          op0=ALU.add, op1=ALU.is_le))
            then(dve.tensor_tensor(second[:], second[:], second_count[:], ALU.mult))
            dve.tensor_tensor(served[:], served[:], second[:], ALU.add).then_inc(served_ready, 1)
            dve.wait_ge(served_ready, 1)
            dve.tensor_tensor(chosen[:].rearrange("p e t -> p t e"), served[:], score[:],
                              ALU.mult).then_inc(chosen_ready, 1)

            def shared(n):
                dve.wait_ge(ab_ready, 2 * n + 2)
                dve.wait_ge(silu_ready, n + 1)
                dve.tensor_tensor(hidden[n][:], silu[n][:], b_ps[n][:], ALU.mult).then_inc(hidden_ready, 1)

            def low_step(n, k):
                dve.wait_ge(hid_hi_ready, n + 1)
                dve.tensor_tensor(hid_lo[k % HBUFS][:], hidden[k % 2][:], hid_hi[k % HBUFS][:].bitcast(F32),
                                  ALU.subtract).then_inc(hid_lo_ready, 1)

            dve.wait_ge(counted, 1)
            dve.tensor_reduce(count8[:], count_ps.rearrange("o (t e) -> o e t", e=EXPERTS), AX_X,
                              ALU.add).then_inc(ordering, 1)
            dve.wait_ge(ordering, 2)
            dve.scalar_tensor_tensor(out=key[:], in0=count8[:], scalar=8.0, in1=falling[:],
                                     op0=ALU.min, op1=ALU.add).then_inc(ordering, 1)
            dve.wait_ge(ordering, 3)
            dve.max(key_sorted[:], key[:]).then_inc(ordering, 1)
            dve.wait_ge(ordering, 4)
            dve.tensor_scalar(used[:], key_sorted[:], 7.5, None, ALU.is_gt).then_inc(ordering, 1)
            dve.tensor_scalar(unkeyed[:], key_sorted[:], -1.0, 7.0, ALU.mult, ALU.add).then_inc(ordering, 1)
            dve.wait_ge(ordering, 6)
            dve.scalar_tensor_tensor(out=order[:, 0:EXPERTS], in0=used[:], scalar=8.0, in1=unkeyed[:],
                                     op0=ALU.mult, op1=ALU.add).then_inc(order_ready, 1)
            dve.tensor_reduce(count8[:, 0:1], used[:].rearrange("o (i k) -> o k i", k=2)[:, 0, :], AX_X,
                              ALU.add).then_inc(ordering, 1)
            dve.wait_ge(ordering, 7)
            dve.tensor_copy(pairs[:], count8[:, 0:1]).then_inc(order_ready, 1)
            shared(0)
            low_step(0, 0)
            shared(1)
            low_step(1, 1)
            running = pairs_to_run(dve)

            def step(n, k, span, former=True):
                dve.wait_ge(ab_ready, n * 2 + 1)
                dve.wait_ge(silu_ready, n - 1)
                dve.tensor_tensor(sa[k % 2][:], a_ps[k % 2][:], span, ALU.mult).then_inc(sa_ready, 1)
                dve.wait_ge(ab_ready, n * 2 + 2)
                dve.tensor_tensor(sbb[k % 2][:], b_ps[k % 2][:], span, ALU.mult).then_inc(sb_ready, 1)
                if former:
                    low_step(n - 1, k - 1)
                dve.wait_ge(silu_ready, n + 1)
                dve.wait_ge(sb_ready, n - 1)
                dve.wait_ge(hid_hi_ready, n - 1)
                dve.tensor_tensor(hidden[k % 2][:], silu[k % 2][:], sbb[k % 2][:],
                                  ALU.mult).then_inc(hidden_ready, 1)

            dve.wait_ge(scale_loaded, 32)
            for n in range(2, 6):
                step(n, n, scale[:, n // 2 - 1, n % 2 * GT:(n % 2 + 1) * GT], former=n > 2)
            with dve.Fori(1, PAIRS) as i:
                with dve.If(running > i):
                    dve.wait_ge(scale_loaded, i * 32 + 32)
                    for k in range(2, 6):
                        span = scale[:, bass.ds(i * 2 + (k // 2 - 1), 1), k % 2 * GT:(k % 2 + 1) * GT]
                        step(i * 4 + k, k, span.rearrange("p o t -> p (o t)"))
            n = running * 4
            low_step(n + 1, 1)
            dve.wait_ge(residual_loaded, 16)
            for g in range(GROUPS):
                for m in range(KT):
                    dve.wait_ge(summed, n * 2 + (2 * g + m + 1))
                    dve.tensor_tensor(result[:, m, g * GT:(g + 1) * GT], out_ps[m][g][:],
                                      residual_sb[:, m, g * GT:(g + 1) * GT], ALU.add).then_inc(result_ready, 1)

        @block.tensor
        def _(pe):
            pe.wait_ge(warm_zeroed, 1)
            for _ in range(WARM_UP):
                pe.matmul(a_ps[0][:], warm[:, 0:P], warm[:], start=True, stop=True)
            for g in range(GROUPS):
                pe.wait_ge(x_loaded[g], 16)
                pe.wait_ge(diag_ready, PER_TILE * (g + 1))
                for t in range(g * GTILES, (g + 1) * GTILES):
                    for m in range(KT):
                        col = (t - g * GTILES) * P
                        last = pe.matmul(out_ps[m][g][:, col:col + P], x_in[:, t, m * P:(m + 1) * P],
                                         cond_diag[:, t, :], start=True, stop=True)
                last.then_inc(mixed_ready, 1)
            pe.wait_ge(gate_hi_ready, 2)
            pe.wait_ge(gate_lo_ready, 2)
            for g in range(GROUPS):
                pe.wait_ge(xt_hi_ready, KT * (g + 1))
                pe.wait_ge(xt_lo_ready, KT * (g + 1))
                passes = [(gv, xv, m) for gv, xv in ((gate_hi, xt_hi), (gate_lo, xt_hi), (gate_hi, xt_lo))
                          for m in range(KT)]
                for i, (gv, xv, m) in enumerate(passes):
                    last = pe.matmul(logit_ps[g][:], gv[:, m, :], xv[:, m, g * GT:(g + 1) * GT],
                                     start=(i == 0), stop=(i == len(passes) - 1))
                last.then_inc(logit_done, 1)
            pe.wait_ge(constants_ready, 5)
            pe.wait_ge(logit_t_ready, GROUPS)
            for t in range(TILES):
                last = pe.transpose(score_ps[:, t * EXPERTS:(t + 1) * EXPERTS], logit_t[:, t * P:(t + 1) * P],
                                    identity[0:EXPERTS, 0:EXPERTS])
            last.then_inc(logit_turned, 1)

            def up_step(turn, k, slot):
                g = k % 2
                if g == 0:
                    pe.wait_ge(w13_hi_ready, turn + 1)
                    pe.wait_ge(w13_lo_ready, turn + 1)
                for which, bank in enumerate((a_ps[k % 2], b_ps[k % 2])):
                    for m in range(KT):
                        col = (m * 2 + which) * HID
                        for i, (wv, xv) in enumerate(((w13_hi, xt_hi), (w13_hi, xt_lo), (w13_lo, xt_hi))):
                            last = pe.matmul(bank[:], wv[slot][:, col:col + HID], xv[:, m, g * GT:(g + 1) * GT],
                                             start=(m == 0 and i == 0), stop=(m == KT - 1 and i == 2))
                    last.then_inc(ab_ready, 1)

            def down_step(turn, n, k, slot, first=False, final=False):
                g = k % 2
                if g == 0:
                    pe.wait_ge(w2_hi_ready, turn + 1)
                    pe.wait_ge(w2_lo_ready, turn + 1)
                pe.wait_ge(hid_hi_ready, n + 1)
                for m in range(KT):
                    for i, (wv, hv) in enumerate(((w2_hi, hid_hi), (w2_lo, hid_hi), (w2_hi, hid_lo))):
                        if m == 0 and i == 2:
                            pe.wait_ge(hid_lo_ready, n + 1)
                        last = pe.matmul(out_ps[m][g][:], wv[slot][:, m * P:(m + 1) * P], hv[k % HBUFS][:],
                                         start=first and i == 0, stop=final and i == 2, skip_group_check=True)
                    last.then_inc(summed, 1)

            up_step(0, 0, 0)
            pe.wait_ge(served_ready, 1)
            pe.matmul(count_ps, eights[:], served[:].rearrange("p t e -> p (t e)"), start=True,
                      stop=True).then_inc(counted, 1)
            pe.wait_ge(chosen_ready, 1)
            pe.transpose(chosen_ps, chosen[:].rearrange("p e t -> p (e t)"), identity[:]).then_inc(chosen_turned, 1)
            pe.wait_ge(chosen_t_ready, 1)
            pe.wait_ge(ordering, 2)
            up_step(0, 1, 0)
            for k in (0, 1):
                down_step(0, k, k, 0, first=True)
            running = pairs_to_run(pe)
            for n in (2, 3):
                up_step(1, n, 1)
            for n in (4, 5):
                pe.wait_ge(sb_ready, n - 3)
                up_step(2, n, 0)
                down_step(1, n - 2, n - 2, 1)
            with pe.Fori(1, PAIRS) as i:
                with pe.If(running > i):
                    turn = i * 2 + 1
                    for k in range(2, 6):
                        n = i * 4 + k
                        pe.wait_ge(sb_ready, n - 3)
                        up_step(turn + (k // 2 - 1), k, k // 2 % 2)
                        down_step(turn + (k // 2 - 2), n - 2, k - 2, (k // 2 - 1) % 2)
            n = running * 4
            for g in range(GROUPS):
                down_step(running * 2, n + g, g, 0, final=True)


def kernel(x, itok_B_1_198, L0_cond_weights, L0_ffn_expert_bias, L0_ffn_gate_w, L0_ffn_w1, L0_ffn_w2, L0_ffn_w3,
           L0_ffn_sw1, L0_ffn_sw2, L0_ffn_sw3):
    import numpy as np
    import concourse.bacc as bacc
    from concourse.bass_utils import run_bass_kernel_spmd

    x = np.asarray(x)
    x_tiles = x.reshape(TILES, P, DIM).transpose(1, 0, 2)
    residual = x.reshape(TOKENS, KT, P).transpose(2, 1, 0)

    def turned(w, sw):
        return np.concatenate([np.asarray(sw)[None], np.asarray(w)]).transpose(2, 0, 1)

    def halves(w):
        return w.reshape(KT, P, EXPERTS + 1, 1, HID).transpose(1, 2, 0, 3, 4)

    w13 = np.concatenate([halves(turned(L0_ffn_w1, L0_ffn_sw1)), halves(turned(L0_ffn_w3, L0_ffn_sw3))], axis=3)
    w2 = turned(L0_ffn_w2, L0_ffn_sw2)
    weights = np.concatenate([w13.reshape(P, EXPERTS + 1, W13), w2], axis=2)
    gate = np.asarray(L0_ffn_gate_w).T.reshape(KT, P, EXPERTS).transpose(1, 0, 2)
    arrays = {
        "x": x_tiles,
        "index": np.asarray(itok_B_1_198).reshape(BATCH, 1),
        "cond_w": np.asarray(L0_cond_weights).reshape(-1, CH * CH),
        "bias": np.asarray(L0_ffn_expert_bias),
        "gate": gate,
        "weights": weights,
        "residual": residual,
    }
    arrays = {name: np.ascontiguousarray(a) for name, a in arrays.items()}
    nc = bacc.Bacc("TRN2", target_bir_lowering=False, num_devices=1)
    args = [nc.dram_tensor(name, a.shape, mybir.dt.from_np(a.dtype), kind="ExternalInput").ap()
            for name, a in arrays.items()]
    scratch = nc.dram_tensor("scratch", (EXPERTS * TILES, P), F32, kind="Internal").ap()
    out = nc.dram_tensor("out", (P, KT, TOKENS), F32, kind="ExternalOutput").ap()
    adaln_ffn_kernel(nc, *args, scratch, out)
    got = run_bass_kernel_spmd(nc, [arrays], core_ids=[0]).results[0]["out"]
    return got.transpose(2, 1, 0).reshape(BATCH, CH, DIM)
```

```python
from contextlib import ExitStack

import concourse.bass as bass
from concourse import mybir

F32 = mybir.dt.float32
F32R = mybir.dt.float32r
BF16 = mybir.dt.bfloat16
I32 = mybir.dt.int32
U32 = mybir.dt.uint32
ALU = mybir.AluOpType
ACT = mybir.ActivationFunctionType
AX_X = mybir.AxisListType.X

P = 128
BATCH, CH, DIM = 32, 32, 256
KT = DIM // P
TOKENS = BATCH * CH
TILES = TOKENS // P
PER_TILE = P // CH
GROUPS = 2
GT = TOKENS // GROUPS
GTILES = TILES // GROUPS
EXPERTS = 8
HID = 128
W1 = KT * HID
W13 = 2 * W1
WCOLS = W13 + DIM
PAIRS = EXPERTS // 2
KEY_BASE = float(2 ** 23)
HBUFS = 4
WARM_UP = 15


def adaln_ffn_kernel(nc, x, index, cond_w, bias, gate, weights, residual, scratch, out):
    with ExitStack() as ctx:
        def sb(name, shape, dt=F32):
            return ctx.enter_context(nc.sbuf_tensor(name, shape, dt))

        def psum(name, shape):
            return ctx.enter_context(nc.psum_tensor(name, shape, F32))

        def sem(name):
            return ctx.enter_context(nc.semaphore(name))

        x_in = sb("x_in", [P, TILES, DIM])
        index_sb = sb("index_sb", [BATCH, 1], I32)
        cond_rows = sb("cond_rows", [BATCH, CH, CH])
        cond_turned = sb("cond_turned", [CH, CH, BATCH])
        cond_diag = sb("cond_diag", [P, TILES, P])
        gate_in = sb("gate_in", [P, KT, EXPERTS])
        gate_split = sb("gate_split", [P, KT, P], F32R)
        logit_t = sb("logit_t", [2 * EXPERTS, TOKENS])
        logit = sb("logit", [P, TILES, EXPERTS])
        score = sb("score", [P, TILES, EXPERTS])
        bias_sb = sb("bias_sb", [P, EXPERTS])
        w_in = sb("w_in", [P, EXPERTS + 1, WCOLS])
        residual_sb = sb("residual_sb", [P, KT, TOKENS])
        xt_hi = sb("xt_hi", [P, KT, TOKENS], F32R)
        xt_lo = sb("xt_lo", [P, KT, TOKENS], F32R)
        w13_hi = [sb(f"w13_hi{i}", [P, W13], F32R) for i in range(2)]
        w13_lo = [sb(f"w13_lo{i}", [P, W13], F32R) for i in range(2)]
        w2_hi = [sb(f"w2_hi{i}", [P, DIM], F32R) for i in range(2)]
        w2_lo = [sb(f"w2_lo{i}", [P, DIM], F32R) for i in range(2)]
        identity = sb("identity", [P, P])
        biased = sb("biased", [P, TILES, EXPERTS])
        top = sb("top", [P, TILES, 8])
        within = sb("within", [P, TILES, EXPERTS])
        second = sb("second", [P, TILES, EXPERTS])
        second_count = sb("second_count", [P, TILES, EXPERTS])
        both = sb("both", [P, TILES])
        served = sb("served", [P, TILES, EXPERTS])
        eights = sb("eights", [P, 1])
        falling_i = sb("falling_i", [1, EXPERTS], I32)
        falling = sb("falling", [1, EXPERTS])
        count8 = sb("count8", [1, EXPERTS])
        key = sb("key", [1, EXPERTS])
        key_sorted = sb("key_sorted", [1, EXPERTS])
        used = sb("used", [1, EXPERTS])
        order = sb("order", [1, 2 * EXPERTS], I32)
        pairs = sb("pairs", [1, 1], I32)
        chosen = sb("chosen", [P, EXPERTS, TILES])
        chosen_t = sb("chosen_t", [EXPERTS * TILES, P])
        scale = sb("scale", [P, EXPERTS, TOKENS])
        sa = [sb(f"sa{i}", [P, GT]) for i in range(2)]
        sbb = [sb(f"sb{i}", [P, GT]) for i in range(2)]
        silu = [sb(f"silu{i}", [P, GT]) for i in range(2)]
        hidden = [sb(f"hidden{i}", [P, GT]) for i in range(2)]
        hid_hi = [sb(f"hid_hi{i}", [P, GT], F32R) for i in range(HBUFS)]
        hid_lo = [sb(f"hid_lo{i}", [P, GT], F32R) for i in range(HBUFS)]
        result = sb("result", [P, KT, TOKENS])
        warm = sb("warm", [P, GT], BF16)
        warm_out = sb("warm_out", [P, 1])

        a_ps = [psum(f"a_ps{i}", [P, GT]) for i in range(2)]
        b_ps = [psum(f"b_ps{i}", [P, GT]) for i in range(2)]
        out_ps = [[psum(f"out_ps{m}{g}", [P, GT]) for g in range(GROUPS)] for m in range(KT)]
        logit_ps = (a_ps[1], b_ps[1])
        logit_turned_ps = out_ps[0][0][:, 0:TILES * 2 * EXPERTS]
        chosen_ps = out_ps[0][1][0:EXPERTS * TILES, 0:P]
        count_ps = out_ps[1][1][0:1, 0:TILES * EXPERTS]

        index_loaded = sem("index_loaded")
        x_loaded = [sem(f"x_loaded{g}") for g in range(GROUPS)]
        gate_loaded = sem("gate_loaded")
        shared_loaded = sem("shared_loaded")
        routed_loaded = sem("routed_loaded")
        residual_loaded = sem("residual_loaded")
        gather_started = sem("gather_started")
        cond_gathered = sem("cond_gathered")
        warm_zeroed = sem("warm_zeroed")
        diag_zeroed = sem("diag_zeroed")
        cond_turned_ready = sem("cond_turned_ready")
        diag_ready = [sem(f"diag_ready{g}") for g in range(GROUPS)]
        constants_blank = sem("constants_blank")
        constants_ready = sem("constants_ready")
        mixed_ready = sem("mixed_ready")
        xt_hi_ready = sem("xt_hi_ready")
        xt_lo_ready = sem("xt_lo_ready")
        gate_zeroed = sem("gate_zeroed")
        gate_hi_ready = sem("gate_hi_ready")
        gate_lo_ready = sem("gate_lo_ready")
        logit_done = sem("logit_done")
        sigmoid_loaded = sem("sigmoid_loaded")
        logit_t_ready = sem("logit_t_ready")
        logit_turned = sem("logit_turned")
        logit_ready = sem("logit_ready")
        score_ready = sem("score_ready")
        routing = sem("routing")
        served_ready = sem("served_ready")
        chosen_ready = sem("chosen_ready")
        chosen_turned = sem("chosen_turned")
        counted = sem("counted")
        ordering = sem("ordering")
        order_ready = sem("order_ready")
        chosen_t_ready = sem("chosen_t_ready")
        scale_written = sem("scale_written")
        scale_loaded = sem("scale_loaded")
        first_scale_loaded = sem("first_scale_loaded")
        ab_ready = sem("ab_ready")
        sa_ready = sem("sa_ready")
        sb_ready = sem("sb_ready")
        silu_ready = sem("silu_ready")
        hidden_ready = sem("hidden_ready")
        hid_hi_ready = sem("hid_hi_ready")
        hid_lo_ready = sem("hid_lo_ready")
        summed = sem("summed")
        w13_hi_ready = sem("w13_hi_ready")
        w13_lo_ready = sem("w13_lo_ready")
        w2_hi_ready = sem("w2_hi_ready")
        w2_lo_ready = sem("w2_lo_ready")
        residual_added = sem("residual_added")
        result_ready = [sem(f"result_ready{m}") for m in range(KT)]
        out_stored = sem("out_stored")

        block = ctx.enter_context(nc.Block())

        def pairs_to_run(engine):
            engine.wait_ge(order_ready, 2)
            return engine.value_load(pairs[0:1, 0:1], min_val=1, max_val=PAIRS)

        def further_pairs(engine, running, body):
            with ExitStack() as nested:
                for i in range(1, PAIRS):
                    nested.enter_context(engine.If(running > i))
                    body(i)

        def expert_of(engine, turn):
            engine.wait_ge(order_ready, 1)
            at = turn - 1
            cell = order[0:1, at:at + 1] if isinstance(at, int) else order[0:1, bass.ds(at, 1)]
            return engine.value_load(cell, min_val=0, max_val=EXPERTS - 1)

        turned = cond_turned[:].rearrange("c d (i j) -> c i d j", j=PER_TILE)

        def diag_block(g, j):
            return cond_diag[j * CH:(j + 1) * CH, g * GTILES:(g + 1) * GTILES, j * CH:(j + 1) * CH]

        @block.sync
        def _(sp):
            sp.dma_start(index_sb[:], index).then_inc(index_loaded, 16)
            sp.dma_start(x_in[:, 0:GTILES, :], x[:, 0:GTILES, :]).then_inc(x_loaded[0], 16)
            sp.wait_ge(gather_started, 1)
            sp.dma_start(x_in[:, GTILES:TILES, :], x[:, GTILES:TILES, :]).then_inc(x_loaded[1], 16)
            sp.dma_start(gate_in[:], gate).then_inc(gate_loaded, 16)
            sp.dma_start(bias_sb[:], bias.partition_broadcast(P)).then_inc(gate_loaded, 16)
            sp.dma_start(w_in[:, 0, :], weights[:, 0, :]).then_inc(shared_loaded, 16)
            for e in (1, 1 + PAIRS):
                sp.dma_start(w_in[:, e:e + PAIRS, :], weights[:, e:e + PAIRS, :]).then_inc(routed_loaded, 16)
            sp.dma_start(residual_sb[:], residual).then_inc(residual_loaded, 16)
            sp.wait_ge(chosen_t_ready, 1)
            sp.dma_start(scratch, chosen_t[:]).then_inc(scale_written, 16)

            rows = scratch.rearrange("(e t) c -> e (t c)", e=EXPERTS)

            def load_scale(turn, cell, loaded):
                e = expert_of(sp, turn)
                sp.dma_start(scale[:, cell, :], rows[bass.ds(e, 1), :].to_broadcast([P, TOKENS])).then_inc(loaded, 16)

            sp.wait_ge(scale_written, 16)
            load_scale(1, 0, first_scale_loaded)
            load_scale(2, 1, scale_loaded)
            running = pairs_to_run(sp)

            def load_scales(i):
                sp.wait_ge(scale_loaded, i * 32 - 16)
                for turn in (i * 2 + 1, i * 2 + 2):
                    load_scale(turn, turn - 1, scale_loaded)

            further_pairs(sp, running, load_scales)
            for g in range(GROUPS):
                for m in range(KT):
                    sp.wait_ge(result_ready[m], g + 1)
                    sp.dma_start(out[:, m, g * GT:(g + 1) * GT],
                                 result[:, m, g * GT:(g + 1) * GT]).then_inc(out_stored, 16)
            sp.wait_ge(out_stored, 16 * GROUPS * KT)

        @block.gpsimd
        def _(pool):
            pool.wait_ge(index_loaded, 16)
            pool.indirect_dma_start(
                out=cond_rows[:].rearrange("b c d -> b (c d)"), out_offset=None,
                in_=cond_w, in_offset=bass.IndirectOffsetOnAxis(ap=index_sb[:].bitcast(U32), axis=0),
                engine_sem=gather_started,
            ).then_inc(cond_gathered, 16)
            pool.memset(identity[:], 0.0).then_inc(constants_blank, 1)
            pool.memset(within[:], 1.0).then_inc(constants_blank, 1)
            pool.memset(eights[:], 8.0).then_inc(constants_ready, 1)
            pool.memset(order[:], 0).then_inc(constants_ready, 1)
            pool.iota(falling_i[:], pattern=[[-1, EXPERTS]], base=EXPERTS - 1,
                      channel_multiplier=0).then_inc(constants_ready, 1)
            pool.wait_ge(constants_blank, 2)
            pool.affine_select(out=identity[:], in_=identity[:], compare_op=ALU.not_equal, fill=1.0,
                               base=0, pattern=[[-1, P]], channel_multiplier=1).then_inc(constants_ready, 1)
            pool.memset(within[:, :, 0:1], 0.0).then_inc(constants_ready, 1)

            def w13_low(turn, slot, source):
                for which in range(2):
                    pool.wait_ge(w13_hi_ready, turn * 2 + which + 1)
                    part = slice(which * W1, (which + 1) * W1)
                    pool.tensor_tensor(w13_lo[slot][:, part], w_in[:, source, part], w13_hi[slot][:, part].bitcast(F32),
                                       ALU.subtract).then_inc(w13_lo_ready, 1)

            def w2_low(turn, slot, source):
                pool.wait_ge(w2_hi_ready, turn + 1)
                pool.tensor_tensor(w2_lo[slot][:], w_in[:, source, W13:WCOLS], w2_hi[slot][:].bitcast(F32),
                                   ALU.subtract).then_inc(w2_lo_ready, 1)

            def pair(turn):
                first, then, next_ = (expert_of(pool, turn + k) for k in range(3))
                w13_low(turn + 1, 0, bass.ds(then + 1, 1))
                w2_low(turn, 1, bass.ds(first + 1, 1))
                w13_low(turn + 2, 1, bass.ds(next_ + 1, 1))
                w2_low(turn + 1, 0, bass.ds(then + 1, 1))

            w13_low(0, 0, 0)
            w2_low(0, 0, 0)
            w13_low(1, 1, bass.ds(expert_of(pool, 1) + 1, 1))
            running = pairs_to_run(pool)
            pair(1)
            further_pairs(pool, running, lambda i: pair(i * 2 + 1))

        @block.scalar
        def _(act):
            def w13_high(slot, source):
                for which in range(2):
                    part = slice(which * W1, (which + 1) * W1)
                    act.copy(w13_hi[slot][:, part], w_in[:, source, part]).then_inc(w13_hi_ready, 1)

            def w2_high(slot, source):
                act.copy(w2_hi[slot][:], w_in[:, source, W13:WCOLS]).then_inc(w2_hi_ready, 1)

            def silu_step(n, k):
                act.wait_ge(sa_ready, n - 1)
                act.wait_ge(hidden_ready, n - 1)
                act.activation(silu[k % 2][:], sa[k % 2][:], ACT.Silu).then_inc(silu_ready, 1)

            def high_step(n, k):
                act.wait_ge(hidden_ready, n + 1)
                act.copy(hid_hi[k % HBUFS][:], hidden[k % 2][:]).then_inc(hid_hi_ready, 1)

            act.wait_ge(warm_zeroed, 1)
            act.activation(warm_out[:], warm[:, 0:1], ACT.Sigmoid).then_inc(sigmoid_loaded, 1)
            act.wait_ge(diag_zeroed, 1)
            act.wait_ge(cond_turned_ready, 1)
            act.copy(diag_block(0, 3), turned[:, 0:GTILES, :, 3]).then_inc(diag_ready[0], 1)
            for j in (2, 3):
                act.copy(diag_block(1, j), turned[:, GTILES:TILES, :, j]).then_inc(diag_ready[1], 1)
            act.wait_ge(gate_loaded, 32)
            act.wait_ge(gate_zeroed, 1)
            act.copy(gate_split[:, :, 0:EXPERTS], gate_in[:]).then_inc(gate_hi_ready, 1)
            act.wait_ge(shared_loaded, 16)
            w13_high(0, 0)
            w2_high(0, 0)
            for g in range(GROUPS):
                for m in range(KT):
                    act.wait_ge(mixed_ready, g * KT + m + 1)
                    act.copy(xt_hi[:, m, g * GT:(g + 1) * GT], out_ps[m][g][:]).then_inc(xt_hi_ready, 1)
            for g in range(GROUPS):
                act.wait_ge(logit_done, g + 1)
                act.copy(logit_t[:, g * GT:(g + 1) * GT], logit_ps[g][0:2 * EXPERTS, :]).then_inc(logit_t_ready, 1)
            act.wait_ge(logit_ready, 1)
            act.activation(score[:], logit[:], ACT.Sigmoid).then_inc(score_ready, 1)
            act.wait_ge(ab_ready, 1)
            act.activation(silu[0][:], a_ps[0][:], ACT.Silu).then_inc(silu_ready, 1)
            high_step(0, 0)
            act.wait_ge(ab_ready, 3)
            act.activation(silu[1][:], a_ps[1][:], ACT.Silu).then_inc(silu_ready, 1)
            act.wait_ge(routed_loaded, 32)
            w13_high(1, bass.ds(expert_of(act, 1) + 1, 1))
            high_step(1, 1)
            running = pairs_to_run(act)

            def pair(turn):
                first, then, next_ = (expert_of(act, turn + k) for k in range(3))
                n = turn * 2
                silu_step(n, 2)
                w13_high(0, bass.ds(then + 1, 1))
                high_step(n, 2)
                w2_high(1, bass.ds(first + 1, 1))
                silu_step(n + 1, 3)
                high_step(n + 1, 3)
                silu_step(n + 2, 4)
                w13_high(1, bass.ds(next_ + 1, 1))
                high_step(n + 2, 4)
                w2_high(0, bass.ds(then + 1, 1))
                silu_step(n + 3, 5)
                high_step(n + 3, 5)

            pair(1)
            further_pairs(act, running, lambda i: pair(i * 2 + 1))
            for g in range(GROUPS):
                act.wait_ge(summed, running * 8 + (2 * g + 1))
                act.copy(result[:, 0, g * GT:(g + 1) * GT], out_ps[0][g][:]).then_inc(result_ready[0], 1)

        @block.vector
        def _(dve):
            dve.memset(warm[:], 0.0).then_inc(warm_zeroed, 1)
            dve.memset(cond_diag[:], 0.0).then_inc(diag_zeroed, 1)
            dve.memset(gate_split[:].bitcast(F32), 0.0).then_inc(gate_zeroed, 1)
            dve.wait_ge(cond_gathered, 16)
            dve.transpose(cond_turned[:], cond_rows[:].rearrange("b c d -> b d c")).then_inc(cond_turned_ready, 1)
            dve.wait_ge(cond_turned_ready, 1)
            dve.wait_ge(diag_zeroed, 1)
            for j in (0, 1, 2):
                dve.tensor_copy(diag_block(0, j), turned[:, 0:GTILES, :, j]).then_inc(diag_ready[0], 1)
            for j in (0, 1):
                dve.tensor_copy(diag_block(1, j), turned[:, GTILES:TILES, :, j]).then_inc(diag_ready[1], 1)
            dve.wait_ge(gate_hi_ready, 1)
            dve.tensor_tensor(gate_split[:, :, EXPERTS:2 * EXPERTS], gate_in[:],
                              gate_split[:, :, 0:EXPERTS].bitcast(F32), ALU.subtract).then_inc(gate_lo_ready, 1)
            dve.wait_ge(constants_ready, 5)
            dve.tensor_scalar(falling[:], falling_i[:], KEY_BASE, None, ALU.add).then_inc(ordering, 1)
            for g in range(GROUPS):
                for m in range(KT):
                    dve.wait_ge(xt_hi_ready, g * KT + m + 1)
                    dve.tensor_tensor(xt_lo[:, m, g * GT:(g + 1) * GT], out_ps[m][g][:],
                                      xt_hi[:, m, g * GT:(g + 1) * GT].bitcast(F32),
                                      ALU.subtract).then_inc(xt_lo_ready, 1)

            steps = [0]

            def then(instruction, done=None):
                steps[0] += 1
                instruction.then_inc(routing, 1)
                dve.wait_ge(routing, steps[0])

            grid = [P, TILES, EXPERTS]
            highest, runner = top[:, :, 0:1], top[:, :, 1:2]
            dve.wait_ge(logit_turned, 1)
            dve.tensor_reduce(logit[:], logit_turned_ps.rearrange("p (t k e) -> p t e k", t=TILES, k=2), AX_X,
                              ALU.add).then_inc(logit_ready, 1)
            dve.wait_ge(score_ready, 1)
            then(dve.tensor_tensor(biased[:], score[:],
                                   bias_sb[:].rearrange("p (o e) -> p o e", o=1).to_broadcast(grid), ALU.add))
            for t in range(TILES):
                last = dve.max(top[:, t, :], biased[:, t, :])
            then(last)
            dve.tensor_tensor(second[:], biased[:], runner.to_broadcast(grid), ALU.is_equal).then_inc(routing, 1)
            dve.tensor_tensor(both[:].rearrange("p (t o) -> p t o", o=1), highest, runner,
                              ALU.is_equal).then_inc(routing, 1)
            dve.tensor_tensor(served[:], biased[:], runner.to_broadcast(grid), ALU.is_gt).then_inc(routing, 1)
            steps[0] += 3
            dve.wait_ge(routing, steps[0])
            then(dve.tensor_tensor_scan(second_count[:].rearrange("p t e -> p (t e)"),
                                        within[:].rearrange("p t e -> p (t e)"),
                                        second[:].rearrange("p t e -> p (t e)"), 0.0, ALU.mult, ALU.add))
            then(dve.scalar_tensor_tensor(out=second_count[:], in0=second_count[:], scalar=-1.0,
                                          in1=both[:].rearrange("p (t o) -> p t o", o=1).to_broadcast(grid),
                                          op0=ALU.add, op1=ALU.is_le))
            then(dve.tensor_tensor(second[:], second[:], second_count[:], ALU.mult))
            dve.tensor_tensor(served[:], served[:], second[:], ALU.add).then_inc(served_ready, 1)
            dve.wait_ge(served_ready, 1)
            dve.tensor_tensor(chosen[:].rearrange("p e t -> p t e"), served[:], score[:],
                              ALU.mult).then_inc(chosen_ready, 1)

            def low_step(n, k):
                dve.wait_ge(hid_hi_ready, n + 1)
                dve.tensor_tensor(hid_lo[k % HBUFS][:], hidden[k % 2][:], hid_hi[k % HBUFS][:].bitcast(F32),
                                  ALU.subtract).then_inc(hid_lo_ready, 1)

            def shared(n):
                dve.wait_ge(ab_ready, 2 * n + 2)
                dve.wait_ge(silu_ready, n + 1)
                dve.tensor_tensor(hidden[n][:], silu[n][:], b_ps[n][:], ALU.mult).then_inc(hidden_ready, 1)

            shared(0)
            dve.wait_ge(counted, 1)
            dve.tensor_reduce(count8[:], count_ps.rearrange("o (t e) -> o e t", e=EXPERTS), AX_X,
                              ALU.add).then_inc(ordering, 1)
            dve.wait_ge(chosen_turned, 1)
            dve.tensor_copy(chosen_t[:], chosen_ps).then_inc(chosen_t_ready, 1)
            dve.wait_ge(ordering, 2)
            dve.scalar_tensor_tensor(out=key[:], in0=count8[:], scalar=8.0, in1=falling[:],
                                     op0=ALU.min, op1=ALU.add).then_inc(ordering, 1)
            dve.wait_ge(ordering, 3)
            dve.max(key_sorted[:], key[:]).then_inc(ordering, 1)
            dve.wait_ge(ordering, 4)
            dve.tensor_scalar(order[:, 0:EXPERTS], key_sorted[:].bitcast(I32), 7, 7, ALU.bitwise_and,
                              ALU.bitwise_xor).then_inc(order_ready, 1)
            low_step(0, 0)
            dve.tensor_scalar(used[:], key_sorted[:], KEY_BASE + 8.0, None, ALU.is_ge).then_inc(ordering, 1)
            dve.wait_ge(ordering, 5)
            dve.tensor_reduce(count8[:, 0:1], used[:].rearrange("o (i k) -> o k i", k=2)[:, 0, :], AX_X,
                              ALU.add).then_inc(ordering, 1)
            dve.wait_ge(ordering, 6)
            dve.tensor_copy(pairs[:], count8[:, 0:1]).then_inc(order_ready, 1)
            shared(1)
            low_step(1, 1)

            def add_residual(m, g):
                dve.wait_ge(summed, 2 * g + m + 1)
                dve.tensor_tensor(out_ps[m][g][:], out_ps[m][g][:], residual_sb[:, m, g * GT:(g + 1) * GT],
                                  ALU.add).then_inc(residual_added, 1)

            dve.wait_ge(residual_loaded, 16)
            for m in range(KT):
                add_residual(m, 0)

            def step(n, k, span):
                dve.wait_ge(ab_ready, n * 2 + 1)
                dve.wait_ge(silu_ready, n - 1)
                dve.tensor_tensor(sa[k % 2][:], a_ps[k % 2][:], span, ALU.mult).then_inc(sa_ready, 1)
                if n % 4 != 2:
                    low_step(n - 1, k - 1)
                dve.wait_ge(ab_ready, n * 2 + 2)
                dve.tensor_tensor(sbb[k % 2][:], b_ps[k % 2][:], span, ALU.mult).then_inc(sb_ready, 1)
                dve.wait_ge(silu_ready, n + 1)
                dve.wait_ge(sb_ready, n - 1)
                dve.tensor_tensor(hidden[k % 2][:], silu[k % 2][:], sbb[k % 2][:],
                                  ALU.mult).then_inc(hidden_ready, 1)
                if n in (2, 3):
                    add_residual(n - 2, 1)
                if n % 4 == 1:
                    low_step(n, k)

            running = pairs_to_run(dve)
            def pair(i):
                for n in range(i * 4 + 2, i * 4 + 6):
                    if n == 2:
                        dve.wait_ge(first_scale_loaded, 16)
                    elif n == 4 or n % 4 == 2:
                        dve.wait_ge(scale_loaded, i * 32 + 16)
                    step(n, n, scale[:, n // 2 - 1, n % 2 * GT:(n % 2 + 1) * GT])

            pair(0)
            further_pairs(dve, running, pair)
            for g in range(GROUPS):
                dve.wait_ge(summed, running * 8 + (2 * g + 2))
                dve.tensor_copy(result[:, 1, g * GT:(g + 1) * GT], out_ps[1][g][:]).then_inc(result_ready[1], 1)

        @block.tensor
        def _(pe):
            pe.wait_ge(warm_zeroed, 1)
            for _ in range(WARM_UP):
                pe.matmul(a_ps[0][:], warm[:, 0:P], warm[:], start=True, stop=True)
            for g in range(GROUPS):
                pe.wait_ge(x_loaded[g], 16)
                pe.wait_ge(diag_ready[g], PER_TILE)
                for m in range(KT):
                    for i in range(GTILES):
                        t = g * GTILES + i
                        last = pe.matmul(out_ps[m][g][:, i * P:(i + 1) * P], x_in[:, t, m * P:(m + 1) * P],
                                         cond_diag[:, t, :], start=True, stop=True)
                    last.then_inc(mixed_ready, 1)
            pe.wait_ge(gate_hi_ready, 1)
            pe.wait_ge(gate_lo_ready, 1)

            def gate_pass(g, m, low):
                xv, ready = ((xt_hi, xt_hi_ready), (xt_lo, xt_lo_ready))[low]
                pe.wait_ge(ready, KT * g + m + 1)
                return pe.matmul(logit_ps[g][:], gate_split[:, m, :], xv[:, m, g * GT:(g + 1) * GT],
                                 start=(m == 0 and not low), stop=(m == KT - 1 and low == 1))

            for m in range(KT):
                for low in range(2):
                    last = gate_pass(0, m, low)
            last.then_inc(logit_done, 1)
            for m, low in ((0, 0), (0, 1), (1, 0)):
                gate_pass(1, m, low)

            def last_gate_pass():
                gate_pass(1, 1, 1).then_inc(logit_done, 1)

            def up_half(turn, k, slot, which, ahead=None):
                g = k % 2
                if g == 0:
                    pe.wait_ge(w13_hi_ready, turn * 2 + which + 1)
                bank = (a_ps, b_ps)[which][k % 2]
                passes = [(w13_hi, xv, m) for m in range(KT) for xv in (xt_hi, xt_lo)]
                passes += [(w13_lo, xt_hi, m) for m in range(KT)]
                for i, (wv, xv, m) in enumerate(passes):
                    if ahead and i in ahead:
                        ahead[i]()
                    if g == 0 and i == 4:
                        pe.wait_ge(w13_lo_ready, turn * 2 + which + 1)
                    col = (which * KT + m) * HID
                    last = pe.matmul(bank[:], wv[slot][:, col:col + HID], xv[:, m, g * GT:(g + 1) * GT],
                                     start=(i == 0), stop=(i == len(passes) - 1))
                last.then_inc(ab_ready, 1)

            def up_step(turn, k, slot):
                up_half(turn, k, slot, 0)
                up_half(turn, k, slot, 1)

            def down_step(turn, n, k, slot, first=False, final=False):
                g = k % 2
                if g == 0:
                    pe.wait_ge(w2_hi_ready, turn + 1)
                    pe.wait_ge(w2_lo_ready, turn + 1)
                pe.wait_ge(hid_hi_ready, n + 1)
                passes = [(wv, hid_hi, m) for m in range(KT) for wv in (w2_hi, w2_lo)]
                if final:
                    passes = passes[0:3] + [(w2_hi, hid_lo, 0)] + passes[3:4] + [(w2_hi, hid_lo, 1)]
                else:
                    passes += [(w2_hi, hid_lo, m) for m in range(KT)]
                for i, (wv, hv, m) in enumerate(passes):
                    if i == (3 if final else 4):
                        pe.wait_ge(hid_lo_ready, n + 1)
                    last = pe.matmul(out_ps[m][g][:], wv[slot][:, m * P:(m + 1) * P], hv[k % HBUFS][:],
                                     start=first and i in (0, 2), stop=final and hv is hid_lo,
                                     skip_group_check=True)
                    if hv is hid_lo:
                        last.then_inc(summed, 1)

            def turn_logits():
                pe.wait_ge(constants_ready, 5)
                pe.wait_ge(logit_t_ready, GROUPS)
                for t in range(TILES):
                    last = pe.transpose(logit_turned_ps[:, t * 2 * EXPERTS:(t + 1) * 2 * EXPERTS],
                                        logit_t[:, t * P:(t + 1) * P], identity[0:2 * EXPERTS, 0:2 * EXPERTS])
                last.then_inc(logit_turned, 1)

            up_half(0, 0, 0, 0, ahead={1: last_gate_pass, 5: turn_logits})
            up_half(0, 0, 0, 1)
            up_half(0, 1, 0, 0)

            def count_tokens():
                pe.wait_ge(served_ready, 1)
                pe.matmul(count_ps, eights[:], served[:].rearrange("p t e -> p (t e)"), start=True,
                          stop=True).then_inc(counted, 1)

            def turn_chosen():
                pe.wait_ge(chosen_ready, 1)
                pe.transpose(chosen_ps, chosen[:].rearrange("p e t -> p (e t)"), identity[:]).then_inc(chosen_turned, 1)

            up_half(0, 1, 0, 1, ahead={2: count_tokens, 3: turn_chosen})
            pe.wait_ge(chosen_t_ready, 1)
            pe.wait_ge(ordering, 2)
            down_step(0, 0, 0, 0, first=True)
            pe.wait_ge(hidden_ready, 1)
            up_step(1, 2, 1)
            down_step(0, 1, 1, 0, first=True)
            pe.wait_ge(hidden_ready, 2)
            up_step(1, 3, 1)
            for n in (4, 5):
                pe.wait_ge(sb_ready, n - 3)
                up_step(2, n, 0)
                pe.wait_ge(residual_added, KT * (n - 3))
                down_step(1, n - 2, n - 2, 1)
            running = pairs_to_run(pe)

            def pair(i):
                for n in range(i * 4 + 2, i * 4 + 6):
                    pe.wait_ge(sb_ready, n - 3)
                    up_step(n // 2, n, n // 2 % 2)
                    down_step(n // 2 - 1, n - 2, n - 2, (n // 2 - 1) % 2)

            further_pairs(pe, running, pair)
            n = running * 4
            for g in range(GROUPS):
                down_step(running * 2, n + g, g, 0, final=True)


def kernel(x, itok_B_1_198, L0_cond_weights, L0_ffn_expert_bias, L0_ffn_gate_w, L0_ffn_w1, L0_ffn_w2, L0_ffn_w3,
           L0_ffn_sw1, L0_ffn_sw2, L0_ffn_sw3):
    import numpy as np
    import concourse.bacc as bacc
    from concourse.bass_utils import run_bass_kernel_spmd

    x = np.asarray(x)
    x_tiles = x.reshape(TILES, P, DIM).transpose(1, 0, 2)
    residual = x.reshape(TOKENS, KT, P).transpose(2, 1, 0)

    def turned(w, sw):
        return np.concatenate([np.asarray(sw)[None], np.asarray(w)]).transpose(2, 0, 1)

    def halves(w):
        return w.reshape(KT, P, EXPERTS + 1, 1, HID).transpose(1, 2, 3, 0, 4)

    w13 = np.concatenate([halves(turned(L0_ffn_w1, L0_ffn_sw1)), halves(turned(L0_ffn_w3, L0_ffn_sw3))], axis=2)
    w2 = turned(L0_ffn_w2, L0_ffn_sw2)
    weights = np.concatenate([w13.reshape(P, EXPERTS + 1, W13), w2], axis=2)
    gate = np.asarray(L0_ffn_gate_w).T.reshape(KT, P, EXPERTS).transpose(1, 0, 2)
    arrays = {
        "x": x_tiles,
        "index": np.asarray(itok_B_1_198).reshape(BATCH, 1),
        "cond_w": np.asarray(L0_cond_weights).reshape(-1, CH * CH),
        "bias": np.asarray(L0_ffn_expert_bias),
        "gate": gate,
        "weights": weights,
        "residual": residual,
    }
    arrays = {name: np.ascontiguousarray(a) for name, a in arrays.items()}
    nc = bacc.Bacc("TRN2", target_bir_lowering=False, num_devices=1)
    args = [nc.dram_tensor(name, a.shape, mybir.dt.from_np(a.dtype), kind="ExternalInput").ap()
            for name, a in arrays.items()]
    scratch = nc.dram_tensor("scratch", (EXPERTS * TILES, P), F32, kind="Internal").ap()
    out = nc.dram_tensor("out", (P, KT, TOKENS), F32, kind="ExternalOutput").ap()
    adaln_ffn_kernel(nc, *args, scratch, out)
    got = run_bass_kernel_spmd(nc, [arrays], core_ids=[0]).results[0]["out"]
    return got.transpose(2, 1, 0).reshape(BATCH, CH, DIM)
```
